# Optimizing a Trainium2 kernel written in Bass

```python
import numpy as np
import jax
import jax.numpy as jnp

def _softmax(x, axis=-1):
    return jax.nn.softmax(x, axis=axis)

def _gelu(x):
    return jax.nn.gelu(x, approximate=True)

def _silu(x):
    return jax.nn.silu(x)

def _sigmoid(x):
    return jax.nn.sigmoid(x)

def _layernorm(x, axis=-1, eps=1e-05):
    m = jnp.mean(x, axis=axis, keepdims=True)
    v = jnp.var(x, axis=axis, keepdims=True)
    return (x - m) / jnp.sqrt(v + eps)

def _scatter_add(tgt, idx, src, axis=0):
    return tgt.at[idx].add(src)

def _segment_sum(src, seg, n):
    return jax.ops.segment_sum(src, seg, n)
kernel_name = 'mk_gnn_resnorm_d1_gnn_r32_52b116'

def setup_inputs(seed: int=0):
    np.random.seed(seed)
    _w = jnp.asarray

    def _rec_inputs():
        import jax
        import jax.numpy as jnp
        _gk = jax.random.key(seed)
        x = -0.000202 + 1 * jax.random.normal(jax.random.fold_in(_gk, 1), (50000, 128), jnp.float32)
        src = jax.random.randint(jax.random.fold_in(_gk, 2), (50000,), 0, 50000, jnp.int32)
        dst = jax.random.randint(jax.random.fold_in(_gk, 3), (50000,), 0, 50000, jnp.int32)
        _o = jnp.argsort(dst, stable=True)
        src = src[_o]
        dst = dst[_o]
        edge_attr_16 = 0.000254156 + 0.999948 * jax.random.normal(jax.random.fold_in(_gk, 11), (50000, 16), jnp.float32)
        return (x, src, dst, edge_attr_16)
    x, src, dst, edge_attr_16 = _rec_inputs()

    def _L0_gnn_setup():
        import jax, jax.numpy as jnp
        import numpy as np
        N = 50000
        E = 25000
        D = 128
        DE = 16
        key = jax.random.key(seed)
        ks = jax.random.split(key, 12)

        def lin(k, fan_in, fan_out):
            bound = 1.0 / np.sqrt(fan_in)
            kw, kb = jax.random.split(k)
            W = jax.random.uniform(kw, (fan_in, fan_out), jnp.float32, -bound, bound)
            b = jax.random.uniform(kb, (fan_out,), jnp.float32, -bound, bound)
            return (W, b)
        x = jax.random.normal(ks[0], (N, D), jnp.float32)
        edge_index = jax.random.randint(ks[1], (2, E), 0, N, jnp.int64)
        edge_attr = jax.random.normal(ks[2], (E, DE), jnp.float32)
        eW1, eb1 = lin(ks[3], 2 * D + DE, D)
        eW2, eb2 = lin(ks[4], D, D)
        nW1, nb1 = lin(ks[5], 2 * D, D)
        nW2, nb2 = lin(ks[6], D, D)
        return {'x': x, 'edge_index': edge_index, 'edge_attr': edge_attr, 'eW1': eW1, 'eb1': eb1, 'eW2': eW2, 'eb2': eb2, 'nW1': nW1, 'nb1': nb1, 'nW2': nW2, 'nb2': nb2}
    _L0_gnn_all = _L0_gnn_setup()
    _L0_gnn_in = {k: v for k, v in _L0_gnn_all.items() if k in ('eW1', 'eb1', 'eW2', 'eb2', 'nW1', 'nb1', 'nW2', 'nb2')}
    del _L0_gnn_all
    return {'x': x, 'src': src, 'dst': dst, 'edge_attr_16': edge_attr_16, 'L0_gnn_eW1': _L0_gnn_in['eW1'], 'L0_gnn_eb1': _L0_gnn_in['eb1'], 'L0_gnn_eW2': _L0_gnn_in['eW2'], 'L0_gnn_eb2': _L0_gnn_in['eb2'], 'L0_gnn_nW1': _L0_gnn_in['nW1'], 'L0_gnn_nb1': _L0_gnn_in['nb1'], 'L0_gnn_nW2': _L0_gnn_in['nW2'], 'L0_gnn_nb2': _L0_gnn_in['nb2']}

def reference(x, src, dst, edge_attr_16, L0_gnn_eW1, L0_gnn_eb1, L0_gnn_eW2, L0_gnn_eb2, L0_gnn_nW1, L0_gnn_nb1, L0_gnn_nW2, L0_gnn_nb2):
    import jax
    import jax.numpy as jnp

    def _L0_gnn_ref(x, edge_index, edge_attr, eW1, eb1, eW2, eb2, nW1, nb1, nW2, nb2):
        import jax, jax.numpy as jnp
        import numpy as np
        N = 50000
        E = 25000
        D = 128
        DE = 16
        row, col = (edge_index[0], edge_index[1])
        edge_input = jnp.concatenate([x[row], x[col], edge_attr], axis=-1)
        h = jax.nn.silu(edge_input @ eW1 + eb1)
        m_ij = jax.nn.silu(h @ eW2 + eb2)
        agg = jax.ops.segment_sum(m_ij, row, num_segments=x.shape[0])
        node_input = jnp.concatenate([x, agg], axis=-1)
        update = jax.nn.silu(node_input @ nW1 + nb1) @ nW2 + nb2
        return x + update
    edge_index = jnp.stack([src, dst])
    x = _layernorm(x + _L0_gnn_ref(x, edge_index, edge_attr_16, L0_gnn_eW1, L0_gnn_eb1, L0_gnn_eW2, L0_gnn_eb2, L0_gnn_nW1, L0_gnn_nb1, L0_gnn_nW2, L0_gnn_nb2), axis=-1)
    return x

_drawn_inputs = setup_inputs


def setup_inputs(seed=0):
    import zlib

    import numpy as np

    out = dict(_drawn_inputs(seed))
    spreads = {}
    factors = {'edge_attr_16': 8.0,
     'L0_gnn_eW1': 8.0,
     'L0_gnn_eb1': 23.045,
     'L0_gnn_eW2': 7.953,
     'L0_gnn_eb2': 54.405,
     'L0_gnn_nb1': 8.0,
     'L0_gnn_nb2': 3.605}
    for name, (base, spread) in spreads.items():
        noise = np.random.default_rng([zlib.crc32(name.encode()), seed]).standard_normal(out[name].shape)
        drawn = base * np.exp(spread * noise) if base else spread * noise
        out[name] = jnp.asarray(drawn.astype(out[name].dtype))
    for name, factor in factors.items():
        out[name] = (out[name] * factor).astype(out[name].dtype)
    return out
```

```python
from contextlib import ExitStack

import concourse.bass as bass
from concourse import mybir

P = 128
D = 128
TILES = 4
GROUP = TILES * P
ROWS = 8
BLOCK = ROWS * P
EPS = 1e-5

F32 = mybir.dt.float32
I32 = mybir.dt.int32
ALU = mybir.AluOpType
ACT = mybir.ActivationFunctionType


def edge_split(E):
    full = E // GROUP
    rest = E - full * GROUP
    return full, TILES - 1, rest // (TILES - 1)


def node_split(N):
    full = N // BLOCK
    rest = N - full * BLOCK
    return full, [(P, 4), ((rest - 4 * P) // 3, 3)]


def gnn_kernel(nc, x, xT, src, gather_idx, attrT, w1s, w1d, w1a, eb1, w2, eb2, nw1a, nb1, nw1b, nw2, nb2, out):
    N = x.shape[0]
    E = src.shape[0]
    DE = attrT.shape[0]
    FULL, LAST_TILES, LAST_P = edge_split(E)
    GROUPS = FULL + 1
    BLOCKS, ENDS = node_split(N)
    SCATTERED_ALL = 16 * (FULL * TILES + LAST_TILES)
    assert FULL % 2 == 1 and BLOCKS % 2 == 0
    assert FULL * GROUP + LAST_TILES * LAST_P == E
    assert BLOCKS * BLOCK + sum(p * r for p, r in ENDS) == N

    table = nc.dram_tensor("table", (N + GROUP, D), F32, kind="Internal").ap()

    with ExitStack() as ctx:
        def sb(name, shape, dt=F32):
            return ctx.enter_context(nc.sbuf_tensor(name, shape, dt))

        def sem(name):
            return ctx.enter_context(nc.semaphore(name))

        psum = [ctx.enter_context(nc.psum_tensor(f"psum{i}", [P, BLOCK], F32)) for i in range(4)]

        w_src, w_dst, w_e2, w_self, w_agg, w_out = (
            sb(n, [P, D]) for n in ("w_src", "w_dst", "w_e2", "w_self", "w_agg", "w_out"))
        w_attr = sb("w_attr", [DE, D])
        b_e1, b_e2 = sb("b_e1", [P, 1]), sb("b_e2", [P, 1])
        b_n1, b_n2 = sb("b_n1", [P, D]), sb("b_n2", [P, D])
        half_n2 = sb("half_n2", [P, D])
        zero = sb("zero", [P, TILES * D])
        ones = sb("ones", [P, P])
        gate_in, gate = sb("gate_in", [1, 1]), sb("gate", [1, 1])
        ident = sb("ident", [P, P])
        earlier = sb("earlier", [P, 2 * P])
        waste_i = sb("waste_i", [P, TILES], I32)
        waste = sb("waste", [P, TILES])
        minus_half = sb("minus_half", [P, ROWS])

        xT_in = [sb(f"xT_in{s}", [P, BLOCK]) for s in range(2)]
        t_new = [sb(f"t_new{s}", [P, BLOCK]) for s in range(2)]
        gidx = [sb(f"gidx{s}", [P, 2 * TILES], I32) for s in range(2)]
        x_src = [sb(f"x_src{s}", [P, TILES * D]) for s in range(2)]
        x_dst = [sb(f"x_dst{s}", [P, TILES * D]) for s in range(2)]
        src_row = [sb(f"src_row{s}", [P, GROUP], I32) for s in range(2)]
        src_col = [sb(f"src_col{s}", [P, TILES], I32) for s in range(2)]
        attr = [sb(f"attr{s}", [DE, GROUP]) for s in range(2)]
        src_f = [sb(f"src_f{s}", [P, TILES]) for s in range(2)]
        xsT = [sb(f"xsT{s}", [P, GROUP]) for s in range(2)]
        xdT = [sb(f"xdT{s}", [P, GROUP]) for s in range(2)]
        hT = [sb(f"hT{s}", [P, GROUP]) for s in range(2)]
        mT = [sb(f"mT{s}", [P, GROUP]) for s in range(2)]
        q = [sb(f"q{s}", [P, GROUP]) for s in range(2)]
        q_sum = [sb(f"q_sum{s}", [P, GROUP]) for s in range(2)]
        same = [sb(f"same{s}", [P, TILES // 2, 3 * P]) for s in range(2)]
        junk = sb("junk", [P, TILES, 2 * P])
        repeats = [sb(f"repeats{s}", [P, TILES]) for s in range(2)]
        to_waste = [sb(f"to_waste{s}", [P, TILES]) for s in range(2)]
        put_off = [sb(f"put_off{s}", [P, TILES]) for s in range(2)]
        sidx = [sb(f"sidx{s}", [P, TILES], I32) for s in range(2)]
        t_in = [sb(f"t_in{s}", [P, BLOCK]) for s in range(2)]
        x_in = [sb(f"x_in{s}", [P, BLOCK]) for s in range(2)]
        uT = [sb(f"uT{s}", [P, BLOCK]) for s in range(2)]
        base = [sb(f"base{s}", [P, BLOCK]) for s in range(2)]
        y = [sb(f"y{s}", [P, BLOCK]) for s in range(2)]
        y_out = [sb(f"y_out{s}", [P, BLOCK]) for s in range(2)]
        stats = [sb(f"stats{s}", [P, ROWS, 6]) for s in range(2)]
        moments = [sb(f"moments{s}", [P, ROWS, 2]) for s in range(2)]
        var_eps = [sb(f"var_eps{s}", [P, ROWS]) for s in range(2)]
        rstd = [sb(f"rstd{s}", [P, ROWS]) for s in range(2)]
        shift = [sb(f"shift{s}", [P, ROWS]) for s in range(2)]

        s_weights = sem("s_weights")
        s_zero, s_ones, s_consts, s_waste_i, s_waste = (
            sem("s_zero"), sem("s_ones"), sem("s_consts"), sem("s_waste_i"), sem("s_waste"))
        s_half_n2, s_gate_in, s_gate = sem("s_half_n2"), sem("s_gate_in"), sem("s_gate")
        s_waste_rows = sem("s_waste_rows")
        s_xT_in = [sem(f"s_xT_in{s}") for s in range(2)]
        s_table_mm, s_t_new = sem("s_table_mm"), sem("s_t_new")
        s_t_stored = [sem(f"s_t_stored{s}") for s in range(2)]
        s_gidx = [sem(f"s_gidx{s}") for s in range(2)]
        s_edge_in = [sem(f"s_edge_in{s}") for s in range(2)]
        s_gathered = [sem(f"s_gathered{s}") for s in range(2)]
        s_src_turned, s_dst_turned = sem("s_src_turned"), sem("s_dst_turned")
        s_xsT, s_xdT = sem("s_xsT"), sem("s_xdT")
        s_h_mm, s_hT, s_m_mm, s_mT = sem("s_h_mm"), sem("s_hT"), sem("s_m_mm"), sem("s_mT")
        s_q_mm, s_q, s_sum_mm, s_q_sum = sem("s_q_mm"), sem("s_q"), sem("s_sum_mm"), sem("s_q_sum")
        s_src_f, s_same, s_repeats, s_put_off, s_sidx = (
            sem("s_src_f"), sem("s_same"), sem("s_repeats"), sem("s_put_off"), sem("s_sidx"))
        s_scattered = sem("s_scattered")
        s_node_in = [sem(f"s_node_in{s}") for s in range(2)]
        s_t_turned, s_uT, s_upd_mm, s_base, s_y = sem("s_t_turned"), sem("s_uT"), sem("s_upd_mm"), sem("s_base"), sem("s_y")
        s_stats, s_moments, s_var_eps, s_rstd, s_y_out = (
            sem("s_stats"), sem("s_moments"), sem("s_var_eps"), sem("s_rstd"), sem("s_y_out"))
        s_shift, s_y_out_act = sem("s_shift"), sem("s_y_out_act")
        s_out = [sem(f"s_out{s}") for s in range(2)]

        WEIGHT_LOADS = 11

        def dve_rows(r):
            return (3 * r) // 8

        def wait(eng, s, value):
            if not isinstance(value, int) or value > 0:
                eng.wait_ge(s, value)

        def blocks(eng, step):
            def at(b, half, s, shape=(P, ROWS), n0=None):
                step(b, half, s, *shape, b * BLOCK if n0 is None else n0)
            for b in range(2):
                at(b, 0, b)
            with eng.Fori(1, BLOCKS // 2) as k:
                for s in range(2):
                    at(k * 2 + s, k, s)
            n0 = BLOCKS * BLOCK
            for b, shape in enumerate(ENDS, BLOCKS):
                at(b, b // 2, b % 2, shape, n0)
                n0 += shape[0] * shape[1]

        def blocks_staggered(eng, first, second):
            def shape(b):
                return (*ENDS[b - BLOCKS], BLOCKS * BLOCK + sum(p * r for p, r in ENDS[:b - BLOCKS])) \
                    if isinstance(b, int) and b >= BLOCKS else (P, ROWS, b * BLOCK)

            def step(b, half, s):
                if not isinstance(b, int) or b + 1 < BLOCKS + len(ENDS):
                    first(b + 1, half + s, 1 - s, *shape(b + 1))
                second(b, half, s, *shape(b))

            first(0, 0, 0, *shape(0))
            for b in range(2):
                step(b, 0, b)
            with eng.Fori(1, BLOCKS // 2 - 1) as k:
                for s in range(2):
                    step(k * 2 + s, k, s)
            for b in range(BLOCKS - 2, BLOCKS + len(ENDS)):
                step(b, b // 2, b % 2)

        def groups(eng, step):
            for g in range(2):
                step(g, 0, g)
            with eng.Fori(1, FULL // 2 - 1) as k:
                for s in range(2):
                    step(k * 2 + s, k, s)
            for g in range(FULL - 3, GROUPS):
                step(g, g // 2, g % 2)

        def shape_of(g):
            return (LAST_TILES, LAST_P) if isinstance(g, int) and g == FULL else (TILES, P)

        def pairs_of(tiles):
            return [[t for t in (a, a + 1) if t < tiles] for a in range(0, tiles, 2)]

        def rows_of(ap, n0, p, r):
            return ap[bass.ds(n0, p * r), :].rearrange("(p r) d -> p (r d)", p=p)

        def mm_view(g_psum):
            return g_psum[:, 0:GROUP], g_psum[:, GROUP:2 * GROUP]

        p_src, p_dst = mm_view(psum[0])
        p_h, p_m = mm_view(psum[1])
        p_q, p_sum = mm_view(psum[2])

        block = ctx.enter_context(nc.Block())

        @block.sync
        def _(sp):
            for dst_sb, src_dram in ((w_self, nw1a), (w_src, w1s), (w_dst, w1d), (w_attr, w1a), (w_e2, w2),
                                     (w_agg, nw1b), (w_out, nw2)):
                sp.dma_start(dst_sb[:], src_dram).then_inc(s_weights, 16)
            for dst_sb, src_dram in ((b_e1, eb1), (b_e2, eb2)):
                sp.dma_start(dst_sb[:], src_dram.rearrange("(p a) -> p a", a=1)).then_inc(s_weights, 16)
            for dst_sb, src_dram in ((b_n1, nb1), (b_n2, nb2)):
                sp.dma_start(dst_sb[:], src_dram.partition_broadcast(P)).then_inc(s_weights, 16)

            sp.wait_ge(s_zero, 1)
            sp.dma_start(rows_of(table, N, P, TILES), zero[:]).then_inc(s_waste_rows, 16)

            def load_gidx(g, half, s):
                wait(sp, s_gathered[s], half * (2 * TILES * 16))
                sp.dma_start(gidx[s][:], gather_idx[g]).then_inc(s_gidx[s], 16)

            load_gidx(0, 0, 0)
            load_gidx(1, 0, 1)

            def load_xT(b, half, s, p, r, n0):
                wait(sp, s_table_mm, b - 1)
                sp.dma_start(xT_in[s][:, 0:p * r], xT[:, bass.ds(n0, p * r)]).then_inc(s_xT_in[s], 16)

            blocks(sp, load_xT)

            def load_edges(g, half, s):
                tiles, p = shape_of(g)
                n = tiles * p
                wait(sp, s_h_mm, g - 1)
                wait(sp, s_sidx, g - 1)
                e0 = g * GROUP
                sp.dma_start(attr[s][:, 0:n], attrT[:, bass.ds(e0, n)]).then_inc(s_edge_in[s], 16)
                sp.dma_start(src_row[s][:, 0:n], src[bass.ds(e0, n)].partition_broadcast(P)).then_inc(s_edge_in[s], 16)
                sp.dma_start(src_col[s][:], gather_idx[g][:, 0:TILES]).then_inc(s_edge_in[s], 16)
                if not isinstance(g, int) or g + 2 < GROUPS:
                    load_gidx(g + 2, half + 1, s)

            groups(sp, load_edges)

            sp.wait_ge(s_scattered, SCATTERED_ALL)

            def load_nodes(b, half, s, p, r, n0):
                wait(sp, s_t_turned, b - 1)
                wait(sp, s_base, b - 1)
                sp.dma_start(t_in[s][0:p, 0:r * D], rows_of(table, n0, p, r)).then_inc(s_node_in[s], 16)
                sp.dma_start(x_in[s][0:p, 0:r * D], rows_of(x, n0, p, r)).then_inc(s_node_in[s], 16)

            blocks(sp, load_nodes)

            ends = BLOCKS + len(ENDS)
            for s in range(2):
                sp.wait_ge(s_out[s], 16 * ((ends - s + 1) // 2))

        @block.gpsimd
        def _(pool):
            pool.memset(zero[:], 0.0).then_inc(s_zero, 1)
            pool.memset(ones[:], 1.0).then_inc(s_ones, 1)
            pool.memset(earlier[:, 0:P], 1.0).then_inc(s_consts, 1)
            pool.memset(minus_half[:], -0.5).then_inc(s_consts, 1)
            pool.memset(gate_in[:], 0.0).then_inc(s_gate_in, 1)
            pool.iota(waste_i[:], [[P, TILES]], base=N, channel_multiplier=1).then_inc(s_waste_i, 1)
            pool.wait_ge(s_zero, 1)
            pool.wait_ge(s_ones, 1)
            pool.affine_select(out=ident[:], in_=zero[:, 0:P], compare_op=ALU.not_equal, fill=1.0, base=0,
                               pattern=[[-1, P]], channel_multiplier=1).then_inc(s_consts, 1)
            pool.affine_select(out=earlier[:, P:2 * P], in_=ones[:], compare_op=ALU.is_gt, fill=0.0, base=0,
                               pattern=[[-1, P]], channel_multiplier=1).then_inc(s_consts, 1)

            def gather(g, half, s, some):
                tiles, p = shape_of(g)
                for t in some:
                    if t >= tiles:
                        continue
                    for rows, col in ((x_src[s], t), (x_dst[s], TILES + t)):
                        pool.indirect_dma_start(
                            rows[0:p, t * D:(t + 1) * D], None, x[:, :],
                            bass.IndirectOffsetOnAxis(ap=gidx[s][0:p, col:col + 1], axis=0),
                        ).then_inc(s_gathered[s], 16)

            def gather_wait(g, half, s):
                wait(pool, s_gidx[s], (half + 1) * 16)
                wait(pool, s_src_turned, g - 1)
                wait(pool, s_dst_turned, g - 1)

            for g in range(2):
                gather_wait(g, 0, g)
                gather(g, 0, g, range(TILES))

            def table_ready():
                for s in range(2):
                    pool.wait_ge(s_t_stored[s], 16 * (BLOCKS // 2 + 1))
                pool.wait_ge(s_waste_rows, 16)
                pool.wait_ge(s_gate_in, 1)

            def step(g, half, s):
                adds = not (isinstance(g, int) and g == 0)
                more = not isinstance(g, int) or g + 2 < GROUPS
                if isinstance(g, int) and g == 1:
                    table_ready()
                if more:
                    gather_wait(g + 2, half + 1, s)
                if adds:
                    wait(pool, s_sidx, g)
                    wait(pool, s_q_sum, g)
                tiles, p = shape_of(g - 1)
                for n, pair in enumerate(pairs_of(TILES)):
                    if adds:
                        wait(pool, s_scattered, (g - 1) * (TILES * 16) + n * 32)
                        wait(pool, s_gate, (g - 1) * 2 + n)
                        pool.tensor_tensor(gate[:], gate_in[:], gate_in[:], ALU.add).then_inc(s_gate, 1)
                        for t in pair:
                            if t < tiles:
                                pool.indirect_dma_start(
                                    table[:, :], bass.IndirectOffsetOnAxis(ap=sidx[1 - s][0:p, t:t + 1], axis=0),
                                    q_sum[1 - s][0:p, t * D:(t + 1) * D], None, compute_op=ALU.add,
                                ).then_inc(s_scattered, 16)
                    if more:
                        gather(g + 2, half + 1, s, pair)

            groups(pool, step)
            step(GROUPS, GROUPS // 2, GROUPS % 2)

            pool.wait_ge(s_half_n2, 1)

            def node(b, half, s, p, r, n0):
                n = r * D
                wait(pool, s_node_in[s], (half + 1) * 32)
                wait(pool, s_y, b - 1)
                bias = half_n2[0:p, :].unsqueeze(1).to_broadcast([p, r, D])
                v = lambda a: a[0:p, 0:n].rearrange("p (r d) -> p r d", r=r)
                pool.tensor_tensor(v(base[s]), v(x_in[s]), bias, ALU.add).then_inc(s_base, 1)

            def node_rstd(b, half, s, p, r, n0):
                wait(pool, s_var_eps, b + 1)
                wait(pool, s_y_out, b - 1)
                wait(pool, s_y_out_act, b - 1)
                pool.tensor_tensor(rstd[s][0:p, 0:r], var_eps[s][0:p, 0:r], minus_half[0:p, 0:r],
                                   ALU.pow).then_inc(s_rstd, 1)

            blocks_staggered(pool, node, node_rstd)

        @block.tensor
        def _(pe):
            pe.wait_ge(s_weights, 16 * WEIGHT_LOADS)

            def table_mm(b, half, s, p, r, n0):
                wait(pe, s_xT_in[s], (half + 1) * 16)
                wait(pe, s_t_new, b - 1)
                for j in range(r):
                    last = nc.tensor.matmul(psum[s][0:p, j * D:(j + 1) * D], xT_in[s][:, j * p:(j + 1) * p], w_self[:],
                                            start=True, stop=True)
                last.then_inc(s_table_mm, 1)

            blocks(pe, table_mm)
            pe.wait_ge(s_t_new, BLOCKS + len(ENDS))
            pe.wait_ge(s_consts, 4)

            def turn(g, half, s):
                tiles, p = shape_of(g)
                wait(pe, s_gathered[s], half * (32 * TILES) + 32 * tiles)
                for rows, ps, read, done in ((x_src[s], p_src, s_xsT, s_src_turned), (x_dst[s], p_dst, s_xdT, s_dst_turned)):
                    wait(pe, read, g)
                    for t in range(tiles):
                        last = nc.tensor.transpose(ps[:, t * p:(t + 1) * p], rows[0:p, t * D:(t + 1) * D], ident[0:p, 0:p])
                    last.then_inc(done, 1)

            def h_mm(g, half, s):
                tiles, p = shape_of(g)
                n = tiles * p
                wait(pe, s_edge_in[s], (half + 1) * 48)
                wait(pe, s_hT, g)
                nc.tensor.matmul(p_h[:, 0:n], w_attr[:], attr[s][:, 0:n], start=True, stop=False)
                wait(pe, s_xsT, g + 1)
                nc.tensor.matmul(p_h[:, 0:n], w_src[:], xsT[s][:, 0:n], start=False, stop=False)
                wait(pe, s_xdT, g + 1)
                nc.tensor.matmul(p_h[:, 0:n], w_dst[:], xdT[s][:, 0:n], start=False, stop=True).then_inc(s_h_mm, 1)

            def m_mm(g, half, s):
                tiles, p = shape_of(g)
                n = tiles * p
                wait(pe, s_mT, g)
                wait(pe, s_hT, g + 1)
                nc.tensor.matmul(p_m[:, 0:n], w_e2[:], hT[s][:, 0:n], start=True, stop=True).then_inc(s_m_mm, 1)

            def q_mm(g, half, s):
                tiles, p = shape_of(g)
                wait(pe, s_q, g)
                wait(pe, s_mT, g + 1)
                for t in range(tiles):
                    last = nc.tensor.matmul(p_q[0:p, t * D:(t + 1) * D], mT[s][:, t * p:(t + 1) * p], w_agg[:],
                                            start=True, stop=True)
                last.then_inc(s_q_mm, 1)

            def step(g, half, s):
                first = isinstance(g, int) and g == 0
                h_mm(g, half, s)
                before = half - 1 if s == 0 else half
                if not first:
                    q_mm(g - 1, before, 1 - s)
                m_mm(g, half, s)
                if not first:
                    sums(g - 1, before, 1 - s)
                if not isinstance(g, int) or g + 1 < GROUPS:
                    turn(g + 1, half + s, 1 - s)

            def sums(g, half, s):
                tiles, p = shape_of(g)
                wait(pe, s_q_sum, g)
                wait(pe, s_same, g + 1)
                wait(pe, s_q, g + 1)
                for n, pair in enumerate(pairs_of(tiles)):
                    a = pair[0]
                    o = p_sum[0:p, a * D:(a + 1) * D]
                    last = nc.tensor.matmul(o, same[s][0:p, n, 0:p], q[s][0:p, a * D:(a + 1) * D],
                                            start=True, stop=len(pair) == 1)
                    if len(pair) == 2:
                        qb = q[s][0:p, (a + 1) * D:(a + 2) * D]
                        nc.tensor.matmul(o, same[s][0:p, n, P:P + p], qb, start=False, stop=True)
                        last = nc.tensor.matmul(p_sum[0:p, (a + 1) * D:(a + 2) * D], same[s][0:p, n, P + p:P + 2 * p], qb,
                                                start=True, stop=True)
                last.then_inc(s_sum_mm, 1)

            turn(0, 0, 0)
            groups(pe, step)
            q_mm(FULL, FULL // 2, FULL % 2)
            sums(FULL, FULL // 2, FULL % 2)

            pe.wait_ge(s_q_sum, GROUPS)

            def turn_t(b, half, s, p, r, n0):
                wait(pe, s_node_in[s], (half + 1) * 32)
                wait(pe, s_uT, b - 1)
                for j in range(r):
                    last = nc.tensor.transpose(psum[s][:, j * p:(j + 1) * p], t_in[s][0:p, j * D:(j + 1) * D], ident[0:p, 0:p])
                last.then_inc(s_t_turned, 1)

            def upd_mm(b, half, s, p, r, n0):
                wait(pe, s_uT, b + 1)
                wait(pe, s_y, b - 1)
                for j in range(r):
                    last = nc.tensor.matmul(psum[2 + s][0:p, j * D:(j + 1) * D], uT[s][:, j * p:(j + 1) * p], w_out[:],
                                            start=True, stop=True)
                last.then_inc(s_upd_mm, 1)

            blocks_staggered(pe, turn_t, upd_mm)

        @block.scalar
        def _(act):
            def store_t(b, half, s, p, r, n0):
                wait(act, s_t_new, b + 1)
                act.dma_start(rows_of(table, n0, p, r), t_new[s][0:p, 0:r * D]).then_inc(s_t_stored[s], 16)

            blocks(act, store_t)
            act.wait_ge(s_weights, 16 * WEIGHT_LOADS)

            def copy_xd(g, half, s):
                tiles, p = shape_of(g)
                n = tiles * p
                wait(act, s_dst_turned, g + 1)
                wait(act, s_h_mm, g - 1)
                nc.scalar.copy(xdT[s][:, 0:n], p_dst[:, 0:n]).then_inc(s_xdT, 1)

            def step(g, half, s):
                tiles, p = shape_of(g)
                n = tiles * p
                wait(act, s_h_mm, g + 1)
                wait(act, s_m_mm, g - 1)
                nc.scalar.activation(hT[s][:, 0:n], p_h[:, 0:n], ACT.Silu, bias=b_e1[:, 0:1]).then_inc(s_hT, 1)
                wait(act, s_m_mm, g + 1)
                wait(act, s_q_mm, g - 1)
                nc.scalar.activation(mT[s][:, 0:n], p_m[:, 0:n], ACT.Silu, bias=b_e2[:, 0:1]).then_inc(s_mT, 1)
                if not isinstance(g, int) or g + 1 < GROUPS:
                    copy_xd(g + 1, half + s, 1 - s)

            copy_xd(0, 0, 0)
            groups(act, step)

            def silu_t(b, half, s, p, r, n0):
                wait(act, s_t_turned, b + 1)
                wait(act, s_upd_mm, b - 1)
                nc.scalar.activation(uT[s][:, 0:p * r], psum[s][:, 0:p * r], ACT.Silu).then_inc(s_uT, 1)

            def scale_out(b, half, s, p, r, n0):
                wait(act, s_shift, b + 1)
                wait(act, s_out[s], half * 16)
                for j in range(dve_rows(r), r):
                    last = nc.scalar.activation(y_out[s][0:p, j * D:(j + 1) * D], y[s][0:p, j * D:(j + 1) * D],
                                                ACT.Identity, bias=shift[s][0:p, j:j + 1], scale=rstd[s][0:p, j:j + 1])
                last.then_inc(s_y_out_act, 1)
                wait(act, s_y_out_act, b + 1)
                wait(act, s_y_out, b + 1)
                act.dma_start(rows_of(out, n0, p, r), y_out[s][0:p, 0:r * D]).then_inc(s_out[s], 16)

            blocks_staggered(act, silu_t, scale_out)

        @block.vector
        def _(dve):
            dve.wait_ge(s_weights, 16 * WEIGHT_LOADS)

            nc.vector.tensor_scalar(half_n2[:], b_n2[:], 0.5, None, ALU.mult).then_inc(s_half_n2, 1)

            def add_nb1(b, half, s, p, r, n0):
                wait(dve, s_table_mm, b + 1)
                wait(dve, s_t_stored[s], half * 16)
                bias = b_n1[0:p, :].unsqueeze(1).to_broadcast([p, r, D])
                v = lambda a: a[0:p, 0:r * D].rearrange("p (r d) -> p r d", r=r)
                nc.vector.tensor_tensor(v(t_new[s]), v(psum[s]), bias, ALU.add).then_inc(s_t_new, 1)

            blocks(dve, add_nb1)

            dve.wait_ge(s_waste_i, 1)
            nc.vector.tensor_copy(waste[:], waste_i[:]).then_inc(s_waste, 1)
            dve.wait_ge(s_waste, 1)
            dve.wait_ge(s_consts, 4)

            def copy_xs(g, half, s):
                tiles, p = shape_of(g)
                n = tiles * p
                wait(dve, s_src_turned, g + 1)
                wait(dve, s_h_mm, g - 1)
                nc.vector.tensor_copy(xsT[s][:, 0:n], p_src[:, 0:n]).then_inc(s_xsT, 1)

            def copy_q(g, half, s):
                tiles, p = shape_of(g)
                wait(dve, s_q_mm, g + 1)
                wait(dve, s_sum_mm, g - 1)
                nc.vector.tensor_copy(q[s][0:p, 0:tiles * D], p_q[0:p, 0:tiles * D]).then_inc(s_q, 1)

            def copy_sum(g, half, s):
                tiles, p = shape_of(g)
                wait(dve, s_sum_mm, g + 1)
                wait(dve, s_scattered, (g - 1) * (16 * TILES))
                nc.vector.tensor_copy(q_sum[s][0:p, 0:tiles * D], p_sum[0:p, 0:tiles * D]).then_inc(s_q_sum, 1)

            def find_same(g, half, s):
                tiles, p = shape_of(g)
                wait(dve, s_edge_in[s], (half + 1) * 48)
                nc.vector.tensor_copy(src_f[s][0:p, 0:tiles], src_col[s][0:p, 0:tiles]).then_inc(s_src_f, 1)
                wait(dve, s_sum_mm, g - 1)
                dve.wait_ge(s_src_f, g + 1)
                for n, pair in enumerate(pairs_of(tiles)):
                    for i, t in enumerate(pair):
                        o = same[s][0:p, n, i * P:i * P + (i + 1) * p]
                        last = nc.vector.tensor_scalar(o, src_row[s][0:p, pair[0] * p:(t + 1) * p],
                                                       src_f[s][0:p, t:t + 1], None, ALU.is_equal)
                last.then_inc(s_same, 1)
                dve.wait_ge(s_same, g + 1)
                nc.vector.tensor_tensor(to_waste[s][0:p, 0:tiles], waste[0:p, 0:tiles], src_f[s][0:p, 0:tiles],
                                        ALU.subtract)
                for n, pair in enumerate(pairs_of(tiles)):
                    for i, t in enumerate(pair):
                        w = (i + 1) * p
                        last = nc.vector.tensor_tensor_reduce(
                            out=junk[0:p, t, 0:w], in0=same[s][0:p, n, i * P:i * P + w],
                            in1=earlier[0:p, P - i * p:P + p], scale=1.0, scalar=0.0, op0=ALU.mult, op1=ALU.add,
                            accum_out=repeats[s][0:p, t:t + 1])
                last.then_inc(s_repeats, 1)
                dve.wait_ge(s_repeats, g + 1)
                nc.vector.scalar_tensor_tensor(out=put_off[s][0:p, 0:tiles], in0=repeats[s][0:p, 0:tiles], scalar=1.0,
                                               in1=to_waste[s][0:p, 0:tiles], op0=ALU.min, op1=ALU.mult
                                               ).then_inc(s_put_off, 1)
                dve.wait_ge(s_put_off, g + 1)
                wait(dve, s_scattered, (g - 1) * (16 * TILES))
                nc.vector.tensor_tensor(sidx[s][0:p, 0:tiles], put_off[s][0:p, 0:tiles], src_f[s][0:p, 0:tiles],
                                        ALU.add).then_inc(s_sidx, 1)

            def step(g, half, s):
                before = half - 1 if s == 0 else half
                if not (isinstance(g, int) and g == 0):
                    copy_q(g - 1, before, 1 - s)
                    copy_sum(g - 1, before, 1 - s)
                find_same(g, half, s)
                if not isinstance(g, int) or g + 1 < GROUPS:
                    copy_xs(g + 1, half + s, 1 - s)

            copy_xs(0, 0, 0)
            groups(dve, step)
            copy_q(FULL, FULL // 2, FULL % 2)
            copy_sum(FULL, FULL // 2, FULL % 2)

            def moments_of(b, half, s, p, r, n0):
                wait(dve, s_upd_mm, b + 1)
                wait(dve, s_base, b + 1)
                wait(dve, s_y_out, b - 1)
                wait(dve, s_y_out_act, b - 1)
                nc.vector.scalar_tensor_tensor(out=y[s][0:p, 0:r * D], in0=base[s][0:p, 0:r * D], scalar=2.0,
                                               in1=psum[2 + s][0:p, 0:r * D], op0=ALU.mult, op1=ALU.add
                                               ).then_inc(s_y, 1)
                dve.wait_ge(s_y, b + 1)
                for j in range(r):
                    last = nc.vector.bn_stats(stats[s][0:p, j, :], y[s][0:p, j * D:(j + 1) * D])
                last.then_inc(s_stats, 1)
                dve.wait_ge(s_half_n2, 1)
                dve.wait_ge(s_stats, b + 1)
                for j in range(r):
                    last = nc.vector.bn_aggr(moments[s][0:p, j, :], stats[s][0:p, j, :])
                last.then_inc(s_moments, 1)
                dve.wait_ge(s_moments, b + 1)
                nc.vector.tensor_scalar(var_eps[s][0:p, 0:r], moments[s][0:p, 0:r, 1], EPS, None, ALU.add
                                        ).then_inc(s_var_eps, 1)

            def normalise(b, half, s, p, r, n0):
                dve.wait_ge(s_rstd, b + 1)
                nc.vector.scalar_tensor_tensor(out=shift[s][0:p, 0:r], in0=moments[s][0:p, 0:r, 0], scalar=-1.0,
                                               in1=rstd[s][0:p, 0:r], op0=ALU.mult, op1=ALU.mult).then_inc(s_shift, 1)
                wait(dve, s_out[s], half * 16)
                for j in range(dve_rows(r)):
                    last = nc.vector.tensor_scalar(y_out[s][0:p, j * D:(j + 1) * D], y[s][0:p, j * D:(j + 1) * D],
                                                   moments[s][0:p, j, 0:1], rstd[s][0:p, j:j + 1],
                                                   ALU.subtract, ALU.mult)
                last.then_inc(s_y_out, 1)

            blocks_staggered(dve, moments_of, normalise)


def kernel(**inputs):
    import numpy as np
    import concourse.bacc as bacc
    from concourse.bass_utils import run_bass_kernel_spmd

    a = {k: np.asarray(v) for k, v in inputs.items()}
    x, src, dst = a["x"], a["src"], a["dst"]
    N, E = x.shape[0], src.shape[0]
    full, last_tiles, last_p = edge_split(E)

    def by_partition(idx):
        o = np.zeros((full + 1, P, TILES), idx.dtype)
        o[:full] = idx[:full * GROUP].reshape(full, TILES, P).transpose(0, 2, 1)
        o[full, :last_p, :last_tiles] = idx[full * GROUP:].reshape(last_tiles, last_p).T
        return o

    blocks, ends = node_split(N)
    parts, n0 = [], 0
    for p, r in [(P, ROWS)] * blocks + ends:
        parts.append(x[n0:n0 + p * r].reshape(p, r, D).transpose(2, 1, 0).reshape(D, p * r))
        n0 += p * r
    eW1, nW1 = a["L0_gnn_eW1"], a["L0_gnn_nW1"]
    arrays = {
        "x_d": x, "xT_d": np.concatenate(parts, axis=1), "src_d": src,
        "gather_idx_d": np.concatenate([by_partition(src), by_partition(dst)], axis=2),
        "attrT_d": a["edge_attr_16"].T,
        "w1s_d": eW1[:D], "w1d_d": eW1[D:2 * D], "w1a_d": eW1[2 * D:], "eb1_d": a["L0_gnn_eb1"],
        "w2_d": a["L0_gnn_eW2"], "eb2_d": a["L0_gnn_eb2"],
        "nw1a_d": nW1[:D], "nb1_d": a["L0_gnn_nb1"], "nw1b_d": nW1[D:],
        "nw2_d": a["L0_gnn_nW2"], "nb2_d": a["L0_gnn_nb2"],
    }
    arrays = {k: np.ascontiguousarray(v) for k, v in arrays.items()}
    nc = bacc.Bacc("TRN2", target_bir_lowering=False, num_devices=1)
    args = [nc.dram_tensor(k, v.shape, mybir.dt.from_np(v.dtype), kind="ExternalInput").ap() for k, v in arrays.items()]
    out = nc.dram_tensor("out", (N, D), F32, kind="ExternalOutput").ap()
    gnn_kernel(nc, *args, out)
    r = run_bass_kernel_spmd(nc, [arrays], core_ids=[0])
    return r.results[0]["out"]
```

```python
from contextlib import ExitStack

import concourse.bass as bass
from concourse import mybir

P = 128
D = 128
TILES = 4
GROUP = TILES * P
ROWS = 8
BLOCK = ROWS * P
WINDOW = 2 * P
EPS = 1e-5

F32 = mybir.dt.float32
I32 = mybir.dt.int32
BF16 = mybir.dt.bfloat16
ALU = mybir.AluOpType
ACT = mybir.ActivationFunctionType
AX = mybir.AxisListType


def edge_split(E):
    full = E // GROUP
    rest = E - full * GROUP
    return full, TILES - 1, rest // (TILES - 1)


def node_split(N):
    full = N // BLOCK
    rest = N - full * BLOCK
    return full, [(P, 4), ((rest - 4 * P) // 3, 3)]


class Group:

    def __init__(self, k, j):
        self.k, self.j = k, j
        self.s, self.s4 = j % 2, j % 4

    @property
    def g(self):
        return self.k * 4 + self.j

    @property
    def half(self):
        return self.k * 2 + self.j // 2

    @property
    def quarter(self):
        return self.k + self.j // 4

    @property
    def known(self):
        return isinstance(self.k, int)

    def next(self, n):
        return Group(self.k, self.j + n)


def gnn_kernel(nc, x, xT, src, dst, gather_idx, attrT, w1s, w1d, w1a, eb1, w2, eb2, nw1a, nb1, nw1b, nw2, nb2, out):
    N = x.shape[0]
    E = src.shape[0]
    DE = attrT.shape[0]
    FULL, LAST_TILES, LAST_P = edge_split(E)
    GROUPS = FULL + 1
    BLOCKS, ENDS = node_split(N)
    SCATTERED_ALL = 16 * (FULL * TILES + LAST_TILES)
    assert FULL % 2 == 1 and BLOCKS % 2 == 0
    assert FULL * GROUP + LAST_TILES * LAST_P == E
    assert BLOCKS * BLOCK + sum(p * r for p, r in ENDS) == N

    table = nc.dram_tensor("table", (N + GROUP, D), F32, kind="Internal").ap()
    place_dram = nc.dram_tensor("place_dram", (GROUPS, GROUP), BF16, kind="Internal").ap()
    first_dram = nc.dram_tensor("first_dram", (FULL, TILES), I32, kind="Internal").ap()

    with ExitStack() as ctx:
        def sb(name, shape, dt=F32):
            return ctx.enter_context(nc.sbuf_tensor(name, shape, dt))

        def sem(name):
            return ctx.enter_context(nc.semaphore(name))

        psum = [ctx.enter_context(nc.psum_tensor(f"psum{i}", [P, BLOCK], F32)) for i in range(4)]

        w_src, w_dst, w_e2, w_self, w_agg, w_out = (
            sb(n, [P, D]) for n in ("w_src", "w_dst", "w_e2", "w_self", "w_agg", "w_out"))
        w_attr = sb("w_attr", [DE, D])
        b_e1, b_e2 = sb("b_e1", [P, 1]), sb("b_e2", [P, 1])
        b_n1, b_n2 = sb("b_n1", [P, D]), sb("b_n2", [P, D])
        half_n2 = sb("half_n2", [P, D])
        zero = sb("zero", [P, TILES * D])
        ones = sb("ones", [P, P])
        ident = sb("ident", [P, P])
        earlier = sb("earlier", [P, 2 * P])
        waste_i = sb("waste_i", [P, TILES], I32)
        waste = sb("waste", [P, TILES])
        minus_half = sb("minus_half", [P, ROWS])

        xT_in = [sb(f"xT_in{s}", [P, BLOCK]) for s in range(2)]
        t_new = [sb(f"t_new{s}", [P, BLOCK]) for s in range(2)]
        gidx = [sb(f"gidx{s}", [P, 2 * TILES], I32) for s in range(4)]
        x_src = [sb(f"x_src{s}", [P, TILES * D]) for s in range(4)]
        window = [sb(f"window{s}", [P, TILES, 2 * D]) for s in range(4)]
        place = [sb(f"place{s}", [P, GROUP], BF16) for s in range(2)]
        pick = [sb(f"pick{s}", [P, 2, GROUP]) for s in range(2)]
        dst_g = sb("dst_g", [FULL, TILES, P], I32)
        dst_min, dst_max, dst_first = (sb(n, [FULL, TILES]) for n in ("dst_min", "dst_max", "dst_first"))
        first_i = sb("first_i", [FULL, TILES], I32)
        first_row = sb("first_row", [1, FULL * TILES], I32)
        reach = sb("reach", [FULL, TILES])
        reach_max, reach_all, fits = sb("reach_max", [P, 1]), sb("reach_all", [P, 1]), sb("fits", [P, 1])
        fits_i = sb("fits_i", [P, 1], I32)
        own_i, own_last_i = sb("own_i", [P, TILES, P], I32), sb("own_last_i", [1, LAST_TILES, LAST_P], I32)
        place_g, off_own = sb("place_g", [FULL, TILES, P]), sb("off_own", [FULL, TILES, P])
        place_b, place_last = sb("place_b", [FULL, TILES, P], BF16), sb("place_last", [1, LAST_TILES, LAST_P], BF16)
        row_i, row_f = sb("row_i", [P, 2], I32), sb("row_f", [P, 2])
        src_row = [sb(f"src_row{s}", [P, GROUP], I32) for s in range(2)]
        src_col = [sb(f"src_col{s}", [P, TILES], I32) for s in range(2)]
        attr = [sb(f"attr{s}", [DE, GROUP]) for s in range(2)]
        src_f = [sb(f"src_f{s}", [P, TILES]) for s in range(2)]
        xsT = [sb(f"xsT{s}", [P, GROUP]) for s in range(2)]
        xdT = [sb(f"xdT{s}", [P, GROUP]) for s in range(2)]
        hT = [sb(f"hT{s}", [P, GROUP]) for s in range(2)]
        mT = [sb(f"mT{s}", [P, GROUP]) for s in range(2)]
        q = [sb(f"q{s}", [P, GROUP]) for s in range(2)]
        q_sum = [sb(f"q_sum{s}", [P, GROUP]) for s in range(2)]
        same = [sb(f"same{s}", [P, TILES // 2, 3 * P]) for s in range(2)]
        junk = sb("junk", [P, TILES, 2 * P])
        repeats = [sb(f"repeats{s}", [P, TILES]) for s in range(2)]
        to_waste = [sb(f"to_waste{s}", [P, TILES]) for s in range(2)]
        put_off = [sb(f"put_off{s}", [P, TILES]) for s in range(2)]
        sidx = [sb(f"sidx{s}", [P, TILES], I32) for s in range(2)]
        t_in = [sb(f"t_in{s}", [P, BLOCK]) for s in range(4)]
        x_in = [sb(f"x_in{s}", [P, BLOCK]) for s in range(4)]
        uT = [sb(f"uT{s}", [P, BLOCK]) for s in range(2)]
        base = [sb(f"base{s}", [P, BLOCK]) for s in range(4)]
        y = [sb(f"y{s}", [P, BLOCK]) for s in range(4)]
        y_out = [sb(f"y_out{s}", [P, BLOCK]) for s in range(4)]
        stats = [sb(f"stats{s}", [P, ROWS, 6]) for s in range(4)]
        moments = [sb(f"moments{s}", [P, ROWS, 2]) for s in range(4)]
        var_eps = [sb(f"var_eps{s}", [P, ROWS]) for s in range(4)]
        rstd = [sb(f"rstd{s}", [P, ROWS]) for s in range(4)]
        shift = [sb(f"shift{s}", [P, ROWS]) for s in range(4)]

        s_weights = sem("s_weights")
        s_zero, s_ones, s_consts, s_waste_i, s_waste = (
            sem("s_zero"), sem("s_ones"), sem("s_consts"), sem("s_waste_i"), sem("s_waste"))
        s_half_n2, s_gate = sem("s_half_n2"), sem("s_gate")
        s_waste_rows = sem("s_waste_rows")
        s_xT_in = [sem(f"s_xT_in{s}") for s in range(2)]
        s_table_mm, s_t_new = sem("s_table_mm"), sem("s_t_new")
        s_t_stored = [sem(f"s_t_stored{s}") for s in range(2)]
        s_gidx = [sem(f"s_gidx{s}") for s in range(4)]
        s_edge_in = [sem(f"s_edge_in{s}") for s in range(2)]
        s_window = [sem(f"s_window{s}") for s in range(4)]
        s_dst_gathered = [sem(f"s_dst_gathered{s}") for s in range(4)]
        s_dst_in = sem("s_dst_in")
        s_place = [sem(f"s_place{s}") for s in range(2)]
        s_dst_g, s_own, s_window_clear, s_range, s_first, s_reach, s_reach_max, s_reach_clear, s_reach_all = (
            sem(n) for n in ("s_dst_g", "s_own", "s_window_clear", "s_range", "s_first", "s_reach", "s_reach_max",
                             "s_reach_clear", "s_reach_all"))
        s_fits, s_fits_i, s_place_g, s_off_own, s_place_b, s_row_f, s_plan, s_first_row, s_pick = (
            sem(n) for n in ("s_fits", "s_fits_i", "s_place_g", "s_off_own", "s_place_b", "s_row_f", "s_plan",
                             "s_first_row", "s_pick"))
        s_gathered = [sem(f"s_gathered{s}") for s in range(4)]
        s_src_turned, s_dst_turned = sem("s_src_turned"), sem("s_dst_turned")
        s_xsT, s_xdT = sem("s_xsT"), sem("s_xdT")
        s_h_mm, s_hT, s_m_mm, s_mT = sem("s_h_mm"), sem("s_hT"), sem("s_m_mm"), sem("s_mT")
        s_q_mm, s_q, s_sum_mm, s_q_sum = sem("s_q_mm"), sem("s_q"), sem("s_sum_mm"), sem("s_q_sum")
        s_src_f, s_same, s_repeats, s_put_off, s_sidx = (
            sem("s_src_f"), sem("s_same"), sem("s_repeats"), sem("s_put_off"), sem("s_sidx"))
        s_scattered = sem("s_scattered")
        s_x_in = [sem(f"s_x_in{s}") for s in range(4)]
        s_t_in = [sem(f"s_t_in{s}") for s in range(4)]
        s_t_turned, s_uT, s_upd_mm, s_base, s_y = sem("s_t_turned"), sem("s_uT"), sem("s_upd_mm"), sem("s_base"), sem("s_y")
        s_stats, s_moments, s_var_eps, s_rstd, s_y_out = (
            sem("s_stats"), sem("s_moments"), sem("s_var_eps"), sem("s_rstd"), sem("s_y_out"))
        s_shift, s_y_out_act = sem("s_shift"), sem("s_y_out_act")
        s_out = [sem(f"s_out{s}") for s in range(4)]

        WEIGHT_LOADS = 11

        def dve_rows(r):
            return max(1, r // 4)

        def wait(eng, s, value):
            if not isinstance(value, int) or value > 0:
                eng.wait_ge(s, value)

        def blocks(eng, step):
            def at(b, half, s, shape=(P, ROWS), n0=None):
                step(b, half, s, *shape, b * BLOCK if n0 is None else n0)
            for b in range(2):
                at(b, 0, b)
            with eng.Fori(1, BLOCKS // 2) as k:
                for s in range(2):
                    at(k * 2 + s, k, s)
            n0 = BLOCKS * BLOCK
            for b, shape in enumerate(ENDS, BLOCKS):
                at(b, b // 2, b % 2, shape, n0)
                n0 += shape[0] * shape[1]

        def blocks_staggered(eng, first, second, lead=1):
            def at(step, b, k, j):
                shape = (P, ROWS, b * BLOCK)
                if isinstance(b, int) and b >= BLOCKS:
                    shape = (*ENDS[b - BLOCKS], BLOCKS * BLOCK + sum(p * r for p, r in ENDS[:b - BLOCKS]))
                step(b, k * 2 + j // 2, k + j // 4, j % 2, j % 4, *shape)

            def both(b, k, j):
                if not isinstance(b, int) or b + lead < BLOCKS + len(ENDS):
                    at(first, b + lead, k, j + lead)
                at(second, b, k, j)

            for b in range(lead):
                at(first, b, 0, b)
            for b in range(4):
                both(b, 0, b)
            with eng.Fori(1, BLOCKS // 4 - 1) as k:
                for j in range(4):
                    both(k * 4 + j, k, j)
            for b in range(BLOCKS - 4, BLOCKS + len(ENDS)):
                both(b, b // 4, b % 4)

        def groups(eng, step):
            for g in range(4):
                step(Group(g // 4, g % 4))
            with eng.Fori(1, FULL // 4 - 1) as k:
                for j in range(4):
                    step(Group(k, j))
            for g in range(FULL // 4 * 4 - 4, GROUPS):
                step(Group(g // 4, g % 4))

        def shape_of(g):
            return (LAST_TILES, LAST_P) if g.known and g.g == FULL else (TILES, P)

        def pairs_of(tiles):
            return [[t for t in (a, a + 1) if t < tiles] for a in range(0, tiles, 2)]

        def rows_of(ap, n0, p, r):
            return ap[bass.ds(n0, p * r), :].rearrange("(p r) d -> p (r d)", p=p)

        def mm_view(g_psum):
            return g_psum[:, 0:GROUP], g_psum[:, GROUP:2 * GROUP]

        p_src, p_dst = mm_view(psum[0])
        p_h, p_m = mm_view(psum[1])
        p_q, p_sum = mm_view(psum[2])

        block = ctx.enter_context(nc.Block())

        @block.sync
        def _(sp):
            sp.dma_start(dst_g[:], dst[0:FULL * GROUP].rearrange("(g t p) -> g t p", t=TILES, p=P)).then_inc(s_dst_g, 16)
            for dst_sb, src_dram in ((w_self, nw1a), (w_src, w1s), (w_dst, w1d), (w_attr, w1a), (w_e2, w2),
                                     (w_agg, nw1b), (w_out, nw2)):
                sp.dma_start(dst_sb[:], src_dram).then_inc(s_weights, 16)
            for dst_sb, src_dram in ((b_e1, eb1), (b_e2, eb2)):
                sp.dma_start(dst_sb[:], src_dram.rearrange("(p a) -> p a", a=1)).then_inc(s_weights, 16)
            for dst_sb, src_dram in ((b_n1, nb1), (b_n2, nb2)):
                sp.dma_start(dst_sb[:], src_dram.partition_broadcast(P)).then_inc(s_weights, 16)

            sp.wait_ge(s_zero, 1)
            sp.dma_start(rows_of(table, N, P, TILES), zero[:]).then_inc(s_waste_rows, 16)

            def load_gidx(g):
                wait(sp, s_gathered[g.s4], g.quarter * (TILES * 16))
                wait(sp, s_dst_in, g.g - 3)
                sp.dma_start(gidx[g.s4][:], gather_idx[g.g]).then_inc(s_gidx[g.s4], 16)

            for g in range(4):
                load_gidx(Group(0, g))

            def load_xT(b, half, s, p, r, n0):
                wait(sp, s_table_mm, b - 1)
                sp.dma_start(xT_in[s][:, 0:p * r], xT[:, bass.ds(n0, p * r)]).then_inc(s_xT_in[s], 16)

            blocks(sp, load_xT)

            sp.wait_ge(s_place_b, 2)
            sp.dma_start(place_dram[0:FULL, :], place_b[:].rearrange("g t p -> g (t p)")).then_inc(s_plan, 16)
            sp.dma_start(place_dram[FULL:GROUPS, 0:LAST_TILES * LAST_P],
                         place_last[:].rearrange("a t p -> a (t p)")).then_inc(s_plan, 16)
            sp.wait_ge(s_first, 2)
            sp.dma_start(first_dram, first_i[:]).then_inc(s_plan, 16)
            sp.wait_ge(s_plan, 48)
            sp.dma_start(first_row[:], first_dram.rearrange("(a g) t -> a (g t)", a=1)).then_inc(s_first_row, 16)
            sp.wait_ge(s_first_row, 16)
            sp.wait_ge(s_window_clear, 4)
            sp.wait_ge(s_fits_i, 1)
            fit = sp.value_load(fits_i[0:1, 0:1], min_val=0, max_val=1)

            def load_place(g):
                wait(sp, s_pick, g.g - 1)
                tiles, p = shape_of(g)
                sp.dma_start(place[g.s][:, 0:tiles * p], place_dram[g.g, 0:tiles * p].partition_broadcast(P)
                             ).then_inc(s_place[g.s], 16)

            def load_windows(g):
                wait(sp, s_dst_turned, g.g - 3)
                for t in range(TILES):
                    at = sp.value_load(first_row[0:1, bass.ds(g.g * TILES + t, 1)], min_val=0, max_val=N - WINDOW)
                    sp.dma_start(window[g.s4][:, t, :], x[bass.ds(at, WINDOW), :].rearrange("(p r) d -> p (r d)", p=P)
                                 ).then_inc(s_window[g.s4], 16)

            def dst_in(windows, g):
                if g.known and g.g == FULL:
                    wait(sp, s_dst_gathered[g.s4], (0 if windows else g.quarter * (16 * TILES)) + 16 * LAST_TILES)
                else:
                    wait(sp, (s_window if windows else s_dst_gathered)[g.s4], (g.quarter + 1) * (16 * TILES))
                sp.sem_inc(s_dst_in, 1)

            def load_edges(windows, g):
                tiles, p = shape_of(g)
                n = tiles * p
                e0 = g.g * GROUP
                wait(sp, s_h_mm, g.g - 1)
                wait(sp, s_same, g.g - 1)
                if not g.known or g.g + 1 < GROUPS:
                    dst_in(windows, g.next(1))
                sp.dma_start(attr[g.s][:, 0:n], attrT[:, bass.ds(e0, n)]).then_inc(s_edge_in[g.s], 16)
                sp.dma_start(src_row[g.s][:, 0:n], src[bass.ds(e0, n)].partition_broadcast(P)).then_inc(s_edge_in[g.s], 16)
                sp.dma_start(src_col[g.s][:], gather_idx[g.g][:, 0:TILES]).then_inc(s_edge_in[g.s], 16)
                if windows and not (g.known and g.g + 3 >= FULL):
                    load_windows(g.next(3))
                if not g.known or g.g + 2 < GROUPS:
                    load_place(g.next(2))
                if not g.known or g.g + 4 < GROUPS:
                    load_gidx(g.next(4))

            def edges(windows):
                for g in range(3):
                    if windows:
                        load_windows(Group(0, g))
                for g in range(2):
                    load_place(Group(0, g))
                dst_in(windows, Group(0, 0))
                groups(sp, lambda g: load_edges(windows, g))

            with sp.If_eq(sp.to_reg(fit), 1):
                edges(True)
            with sp.Else():
                edges(False)

            def load_x(b, half, quarter, s, s4, p, r, n0):
                wait(sp, s_base, b - 3)
                sp.dma_start(x_in[s4][0:p, 0:r * D], rows_of(x, n0, p, r)).then_inc(s_x_in[s4], 16)

            def load_t(b, half, quarter, s, s4, p, r, n0):
                if isinstance(b, int) and b == 0:
                    sp.wait_ge(s_scattered, SCATTERED_ALL)
                wait(sp, s_t_turned, b - 3)
                sp.dma_start(t_in[s4][0:p, 0:r * D], rows_of(table, n0, p, r)).then_inc(s_t_in[s4], 16)

            blocks_staggered(sp, load_x, load_t)

            for s4 in range(4):
                sp.wait_ge(s_out[s4], 16 * ((BLOCKS + len(ENDS) - s4 + 3) // 4))

        @block.gpsimd
        def _(pool):
            pool.memset(zero[:], 0.0).then_inc(s_zero, 1)
            pool.memset(ones[:], 1.0).then_inc(s_ones, 1)
            pool.memset(earlier[:, 0:P], 1.0).then_inc(s_consts, 1)
            pool.memset(minus_half[:], -0.5).then_inc(s_consts, 1)
            pool.memset(reach_max[:], 0.0).then_inc(s_reach_clear, 1)
            pool.iota(own_i[:], [[0, TILES], [2, P]], base=0, channel_multiplier=0).then_inc(s_own, 1)
            pool.iota(own_last_i[:], [[0, LAST_TILES], [2, LAST_P]], base=0, channel_multiplier=0).then_inc(s_own, 1)
            pool.iota(row_i[:], [[1, 2]], base=0, channel_multiplier=2).then_inc(s_own, 1)
            for s in range(4):
                pool.memset(window[s][:], 0.0).then_inc(s_window_clear, 1)
            pool.iota(waste_i[:], [[P, TILES]], base=N, channel_multiplier=1).then_inc(s_waste_i, 1)
            pool.wait_ge(s_zero, 1)
            pool.wait_ge(s_ones, 1)
            pool.affine_select(out=ident[:], in_=zero[:, 0:P], compare_op=ALU.not_equal, fill=1.0, base=0,
                               pattern=[[-1, P]], channel_multiplier=1).then_inc(s_consts, 1)
            pool.affine_select(out=earlier[:, P:2 * P], in_=ones[:], compare_op=ALU.is_gt, fill=0.0, base=0,
                               pattern=[[-1, P]], channel_multiplier=1).then_inc(s_consts, 1)

            pool.wait_ge(s_reach_max, 1)
            pool.partition_all_reduce(reach_all[:], reach_max[:], P, bass.bass_isa.ReduceOp.max).then_inc(s_reach_all, 1)
            pool.wait_ge(s_window_clear, 4)

            def gather_rows(rows, g, p, col, done):
                pool.indirect_dma_start(
                    rows, None, x[:, :], bass.IndirectOffsetOnAxis(ap=gidx[g.s4][0:p, col:col + 1], axis=0)
                ).then_inc(done[g.s4], 16)

            def gather(windows, g, some):
                tiles, p = shape_of(g)
                for t in some:
                    if t >= tiles:
                        continue
                    gather_rows(x_src[g.s4][0:p, t * D:(t + 1) * D], g, p, t, s_gathered)
                    if not windows or (g.known and g.g == FULL):
                        gather_rows(window[g.s4][0:p, t, 0:D], g, p, TILES + t, s_dst_gathered)

            def gather_wait(windows, g):
                wait(pool, s_gidx[g.s4], (g.quarter + 1) * 16)
                wait(pool, s_src_turned, g.g - 3)
                if not windows or (g.known and g.g == FULL):
                    wait(pool, s_dst_turned, g.g - 3)

            pool.wait_ge(s_fits_i, 1)
            fit = pool.value_load(fits_i[0:1, 0:1], min_val=0, max_val=1)

            def table_ready():
                for s in range(2):
                    pool.wait_ge(s_t_stored[s], 16 * (BLOCKS // 2 + 1))
                pool.wait_ge(s_waste_rows, 16)

            def step(windows, g):
                adds = not g.known or g.g >= 2
                more = not g.known or g.g + 3 < GROUPS
                if more:
                    gather_wait(windows, g.next(3))
                if adds:
                    wait(pool, s_sidx, g.g - 1)
                    wait(pool, s_q_sum, g.g - 1)
                tiles, p = shape_of(g.next(-2))
                for n, pair in enumerate(pairs_of(TILES)):
                    if adds:
                        wait(pool, s_scattered, (g.g - 2) * (TILES * 16) + n * 32)
                        pool.sem_inc(s_gate, 1)
                        for t in pair:
                            if t < tiles:
                                pool.indirect_dma_start(
                                    table[:, :], bass.IndirectOffsetOnAxis(ap=sidx[g.s][0:p, t:t + 1], axis=0),
                                    q_sum[g.s][0:p, t * D:(t + 1) * D], None, compute_op=ALU.add,
                                ).then_inc(s_scattered, 16)
                    if more:
                        gather(windows, g.next(3), pair)
                if g.known and g.g == 1:
                    table_ready()

            def edges(windows):
                for g in range(3):
                    gather_wait(windows, Group(0, g))
                    gather(windows, Group(0, g), range(TILES))
                groups(pool, lambda g: step(windows, g))
                for g in (GROUPS, GROUPS + 1):
                    step(windows, Group(g // 4, g % 4))

            with pool.If_eq(pool.to_reg(fit), 1):
                edges(True)
            with pool.Else():
                edges(False)

            pool.wait_ge(s_half_n2, 1)

            def node(b, half, quarter, s, s4, p, r, n0):
                n = r * D
                wait(pool, s_x_in[s4], (quarter + 1) * 16)
                wait(pool, s_y, b - 3)
                bias = half_n2[0:p, :].unsqueeze(1).to_broadcast([p, r, D])
                v = lambda a: a[0:p, 0:n].rearrange("p (r d) -> p r d", r=r)
                pool.tensor_tensor(v(base[s4]), v(x_in[s4]), bias, ALU.add).then_inc(s_base, 1)

            def node_rstd(b, half, quarter, s, s4, p, r, n0):
                wait(pool, s_var_eps, b + 1)
                wait(pool, s_y_out, b - 3)
                wait(pool, s_y_out_act, b - 3)
                pool.tensor_tensor(rstd[s4][0:p, 0:r], var_eps[s4][0:p, 0:r], minus_half[0:p, 0:r],
                                   ALU.pow).then_inc(s_rstd, 1)

            blocks_staggered(pool, node, node_rstd, lead=2)

        @block.tensor
        def _(pe):
            pe.wait_ge(s_weights, 16 * WEIGHT_LOADS)

            def table_mm(b, half, s, p, r, n0):
                wait(pe, s_xT_in[s], (half + 1) * 16)
                wait(pe, s_t_new, b - 1)
                for j in range(r):
                    last = nc.tensor.matmul(psum[s][0:p, j * D:(j + 1) * D], xT_in[s][:, j * p:(j + 1) * p], w_self[:],
                                            start=True, stop=True)
                last.then_inc(s_table_mm, 1)

            blocks(pe, table_mm)
            pe.wait_ge(s_t_new, BLOCKS + len(ENDS))
            pe.wait_ge(s_consts, 4)

            def turn(g):
                tiles, p = shape_of(g)
                wait(pe, s_gathered[g.s4], g.quarter * (16 * TILES) + 16 * tiles)
                wait(pe, s_xsT, g.g)
                for t in range(tiles):
                    last = nc.tensor.transpose(p_src[:, t * p:(t + 1) * p], x_src[g.s4][0:p, t * D:(t + 1) * D], ident[0:p, 0:p])
                last.then_inc(s_src_turned, 1)
                wait(pe, s_dst_in, g.g + 1)
                wait(pe, s_pick, g.g + 1)
                wait(pe, s_xdT, g.g)
                for t in range(tiles):
                    for r in range(2):
                        last = nc.tensor.matmul(p_dst[:, t * p:(t + 1) * p], window[g.s4][:, t, r * D:(r + 1) * D],
                                                pick[g.s][:, r, t * p:(t + 1) * p], start=r == 0, stop=r == 1)
                last.then_inc(s_dst_turned, 1)

            def h_mm(g):
                tiles, p = shape_of(g)
                n = tiles * p
                wait(pe, s_edge_in[g.s], (g.half + 1) * 48)
                wait(pe, s_hT, g.g)
                nc.tensor.matmul(p_h[:, 0:n], w_attr[:], attr[g.s][:, 0:n], start=True, stop=False)
                wait(pe, s_xsT, g.g + 1)
                nc.tensor.matmul(p_h[:, 0:n], w_src[:], xsT[g.s][:, 0:n], start=False, stop=False)
                wait(pe, s_xdT, g.g + 1)
                nc.tensor.matmul(p_h[:, 0:n], w_dst[:], xdT[g.s][:, 0:n], start=False, stop=True).then_inc(s_h_mm, 1)

            def m_mm(g):
                tiles, p = shape_of(g)
                n = tiles * p
                wait(pe, s_mT, g.g)
                wait(pe, s_hT, g.g + 1)
                nc.tensor.matmul(p_m[:, 0:n], w_e2[:], hT[g.s][:, 0:n], start=True, stop=True).then_inc(s_m_mm, 1)

            def q_mm(g):
                tiles, p = shape_of(g)
                wait(pe, s_q, g.g)
                wait(pe, s_mT, g.g + 1)
                for t in range(tiles):
                    last = nc.tensor.matmul(p_q[0:p, t * D:(t + 1) * D], mT[g.s][:, t * p:(t + 1) * p], w_agg[:],
                                            start=True, stop=True)
                last.then_inc(s_q_mm, 1)

            def step(g):
                h_mm(g)
                if not g.known or g.g + 1 < GROUPS:
                    turn(g.next(1))
                m_mm(g)
                if not g.known or g.g > 0:
                    sums(g.next(-1))
                q_mm(g)

            def sums(g):
                tiles, p = shape_of(g)
                wait(pe, s_q_sum, g.g)
                wait(pe, s_same, g.g + 1)
                wait(pe, s_q, g.g + 1)
                for n, pair in enumerate(pairs_of(tiles)):
                    a = pair[0]
                    o = p_sum[0:p, a * D:(a + 1) * D]
                    last = nc.tensor.matmul(o, same[g.s][0:p, n, 0:p], q[g.s][0:p, a * D:(a + 1) * D],
                                            start=True, stop=len(pair) == 1)
                    if len(pair) == 2:
                        qb = q[g.s][0:p, (a + 1) * D:(a + 2) * D]
                        nc.tensor.matmul(o, same[g.s][0:p, n, P:P + p], qb, start=False, stop=True)
                        last = nc.tensor.matmul(p_sum[0:p, (a + 1) * D:(a + 2) * D], same[g.s][0:p, n, P + p:P + 2 * p], qb,
                                                start=True, stop=True)
                last.then_inc(s_sum_mm, 1)

            turn(Group(0, 0))
            groups(pe, step)
            sums(Group(FULL // 4, FULL % 4))

            pe.wait_ge(s_q_sum, GROUPS)

            def turn_t(b, half, quarter, s, s4, p, r, n0):
                wait(pe, s_t_in[s4], (quarter + 1) * 16)
                wait(pe, s_uT, b - 1)
                for j in range(r):
                    last = nc.tensor.transpose(psum[s][:, j * p:(j + 1) * p], t_in[s4][0:p, j * D:(j + 1) * D], ident[0:p, 0:p])
                last.then_inc(s_t_turned, 1)

            def upd_mm(b, half, quarter, s, s4, p, r, n0):
                wait(pe, s_uT, b + 1)
                wait(pe, s_y, b - 1)
                for j in range(r):
                    last = nc.tensor.matmul(psum[2 + s][0:p, j * D:(j + 1) * D], uT[s][:, j * p:(j + 1) * p], w_out[:],
                                            start=True, stop=True)
                last.then_inc(s_upd_mm, 1)

            blocks_staggered(pe, turn_t, upd_mm)

        @block.scalar
        def _(act):
            def store_t(b, half, s, p, r, n0):
                wait(act, s_t_new, b + 1)
                act.dma_start(rows_of(table, n0, p, r), t_new[s][0:p, 0:r * D]).then_inc(s_t_stored[s], 16)

            blocks(act, store_t)
            act.wait_ge(s_weights, 16 * WEIGHT_LOADS)

            def copy_xd(g):
                tiles, p = shape_of(g)
                n = tiles * p
                wait(act, s_dst_turned, g.g + 1)
                wait(act, s_h_mm, g.g - 1)
                nc.scalar.copy(xdT[g.s][:, 0:n], p_dst[:, 0:n]).then_inc(s_xdT, 1)

            def step(g):
                tiles, p = shape_of(g)
                n = tiles * p
                wait(act, s_h_mm, g.g + 1)
                wait(act, s_m_mm, g.g - 1)
                nc.scalar.activation(hT[g.s][:, 0:n], p_h[:, 0:n], ACT.Silu, bias=b_e1[:, 0:1]).then_inc(s_hT, 1)
                if not g.known or g.g + 1 < GROUPS:
                    copy_xd(g.next(1))
                wait(act, s_m_mm, g.g + 1)
                wait(act, s_q_mm, g.g - 1)
                nc.scalar.activation(mT[g.s][:, 0:n], p_m[:, 0:n], ACT.Silu, bias=b_e2[:, 0:1]).then_inc(s_mT, 1)

            copy_xd(Group(0, 0))
            groups(act, step)

            def silu_t(b, half, quarter, s, s4, p, r, n0):
                wait(act, s_t_turned, b + 1)
                wait(act, s_upd_mm, b - 1)
                nc.scalar.activation(uT[s][:, 0:p * r], psum[s][:, 0:p * r], ACT.Silu).then_inc(s_uT, 1)

            def scale_out(b, half, quarter, s, s4, p, r, n0):
                wait(act, s_shift, b + 1)
                wait(act, s_out[s4], quarter * 16)
                for j in range(dve_rows(r), r):
                    last = nc.scalar.activation(y_out[s4][0:p, j * D:(j + 1) * D], y[s4][0:p, j * D:(j + 1) * D],
                                                ACT.Identity, bias=shift[s4][0:p, j:j + 1], scale=rstd[s4][0:p, j:j + 1])
                last.then_inc(s_y_out_act, 1)
                wait(act, s_y_out_act, b + 1)
                wait(act, s_y_out, b + 1)
                act.dma_start(rows_of(out, n0, p, r), y_out[s4][0:p, 0:r * D]).then_inc(s_out[s4], 16)

            blocks_staggered(act, silu_t, scale_out, lead=3)

        @block.vector
        def _(dve):
            def plan_windows():
                dve.wait_ge(s_dst_g, 16)
                nc.vector.tensor_reduce(dst_min[:], dst_g[:], AX.X, ALU.min)
                nc.vector.tensor_reduce(dst_max[:], dst_g[:], AX.X, ALU.max).then_inc(s_range, 1)
                dve.wait_ge(s_range, 1)
                nc.vector.tensor_scalar(dst_first[:], dst_min[:], float(N - WINDOW), None, ALU.min).then_inc(s_first, 1)
                dve.wait_ge(s_first, 1)
                nc.vector.tensor_copy(first_i[:], dst_first[:]).then_inc(s_first, 1)
                nc.vector.tensor_tensor(reach[:], dst_max[:], dst_first[:], ALU.subtract).then_inc(s_reach, 1)
                dve.wait_ge(s_reach, 1)
                dve.wait_ge(s_reach_clear, 1)
                nc.vector.tensor_reduce(reach_max[0:FULL, :], reach[:], AX.X, ALU.max).then_inc(s_reach_max, 1)
                dve.wait_ge(s_own, 3)
                nc.vector.tensor_copy(row_f[:], row_i[:]).then_inc(s_row_f, 1)
                nc.vector.tensor_copy(place_last[:], own_last_i[:]).then_inc(s_place_b, 1)
                nc.vector.tensor_tensor(place_g[:], dst_g[:], dst_first[:].unsqueeze(2).to_broadcast([FULL, TILES, P]),
                                        ALU.subtract).then_inc(s_place_g, 1)
                dve.wait_ge(s_place_g, 1)
                nc.vector.tensor_tensor(off_own[:], place_g[:], own_i[0:FULL], ALU.subtract).then_inc(s_off_own, 1)
                dve.wait_ge(s_reach_all, 1)
                nc.vector.tensor_scalar(fits[:], reach_all[:], float(WINDOW - 1), None, ALU.is_le).then_inc(s_fits, 1)
                dve.wait_ge(s_fits, 1)
                nc.vector.tensor_copy(fits_i[:], fits[:]).then_inc(s_fits_i, 1)
                dve.wait_ge(s_off_own, 1)
                nc.vector.scalar_tensor_tensor(out=place_b[:], in0=off_own[:], scalar=fits[0:FULL, 0:1],
                                               in1=own_i[0:FULL], op0=ALU.mult, op1=ALU.add).then_inc(s_place_b, 1)
                dve.wait_ge(s_row_f, 1)

            dve.wait_ge(s_weights, 16 * WEIGHT_LOADS)

            plan_windows()
            nc.vector.tensor_scalar(half_n2[:], b_n2[:], 0.5, None, ALU.mult).then_inc(s_half_n2, 1)

            def add_nb1(b, half, s, p, r, n0):
                wait(dve, s_table_mm, b + 1)
                wait(dve, s_t_stored[s], half * 16)
                bias = b_n1[0:p, :].unsqueeze(1).to_broadcast([p, r, D])
                v = lambda a: a[0:p, 0:r * D].rearrange("p (r d) -> p r d", r=r)
                nc.vector.tensor_tensor(v(t_new[s]), v(psum[s]), bias, ALU.add).then_inc(s_t_new, 1)

            blocks(dve, add_nb1)

            dve.wait_ge(s_waste_i, 1)
            nc.vector.tensor_copy(waste[:], waste_i[:]).then_inc(s_waste, 1)
            dve.wait_ge(s_waste, 1)
            dve.wait_ge(s_consts, 4)

            def copy_xs(g):
                tiles, p = shape_of(g)
                n = tiles * p
                wait(dve, s_src_turned, g.g + 1)
                wait(dve, s_h_mm, g.g - 1)
                nc.vector.tensor_copy(xsT[g.s][:, 0:n], p_src[:, 0:n]).then_inc(s_xsT, 1)

            def copy_q(g):
                tiles, p = shape_of(g)
                wait(dve, s_q_mm, g.g + 1)
                wait(dve, s_sum_mm, g.g - 1)
                nc.vector.tensor_copy(q[g.s][0:p, 0:tiles * D], p_q[0:p, 0:tiles * D]).then_inc(s_q, 1)

            def copy_sum(g):
                tiles, p = shape_of(g)
                wait(dve, s_sum_mm, g.g + 1)
                wait(dve, s_scattered, (g.g - 1) * (16 * TILES))
                nc.vector.tensor_copy(q_sum[g.s][0:p, 0:tiles * D], p_sum[0:p, 0:tiles * D]).then_inc(s_q_sum, 1)

            def find_same(g):
                tiles, p = shape_of(g)
                wait(dve, s_edge_in[g.s], (g.half + 1) * 48)
                wait(dve, s_sidx, g.g - 1)
                nc.vector.tensor_copy(src_f[g.s][0:p, 0:tiles], src_col[g.s][0:p, 0:tiles]).then_inc(s_src_f, 1)
                wait(dve, s_sum_mm, g.g - 1)
                dve.wait_ge(s_src_f, g.g + 1)
                for n, pair in enumerate(pairs_of(tiles)):
                    for i, t in enumerate(pair):
                        o = same[g.s][0:p, n, i * P:i * P + (i + 1) * p]
                        last = nc.vector.tensor_scalar(o, src_row[g.s][0:p, pair[0] * p:(t + 1) * p],
                                                       src_f[g.s][0:p, t:t + 1], None, ALU.is_equal)
                last.then_inc(s_same, 1)

            def find_repeats(g):
                tiles, p = shape_of(g)
                dve.wait_ge(s_same, g.g + 1)
                nc.vector.tensor_tensor(to_waste[g.s][0:p, 0:tiles], waste[0:p, 0:tiles], src_f[g.s][0:p, 0:tiles],
                                        ALU.subtract)
                for n, pair in enumerate(pairs_of(tiles)):
                    for i, t in enumerate(pair):
                        w = (i + 1) * p
                        last = nc.vector.tensor_tensor_reduce(
                            out=junk[0:p, t, 0:w], in0=same[g.s][0:p, n, i * P:i * P + w],
                            in1=earlier[0:p, P - i * p:P + p], scale=1.0, scalar=0.0, op0=ALU.mult, op1=ALU.add,
                            accum_out=repeats[g.s][0:p, t:t + 1])
                last.then_inc(s_repeats, 1)
                dve.wait_ge(s_repeats, g.g + 1)
                nc.vector.scalar_tensor_tensor(out=put_off[g.s][0:p, 0:tiles], in0=repeats[g.s][0:p, 0:tiles], scalar=1.0,
                                               in1=to_waste[g.s][0:p, 0:tiles], op0=ALU.min, op1=ALU.mult
                                               ).then_inc(s_put_off, 1)

            def place_sums(g):
                tiles, p = shape_of(g)
                dve.wait_ge(s_put_off, g.g + 1)
                wait(dve, s_scattered, (g.g - 1) * (16 * TILES))
                nc.vector.tensor_tensor(sidx[g.s][0:p, 0:tiles], put_off[g.s][0:p, 0:tiles], src_f[g.s][0:p, 0:tiles],
                                        ALU.add).then_inc(s_sidx, 1)

            def make_pick(g):
                tiles, p = shape_of(g)
                n = tiles * p
                wait(dve, s_place[g.s], (g.half + 1) * 16)
                wait(dve, s_dst_turned, g.g - 1)
                for r in range(2):
                    last = nc.vector.tensor_scalar(pick[g.s][:, r, 0:n], place[g.s][:, 0:n], row_f[:, r:r + 1], None,
                                                   ALU.is_equal)
                last.then_inc(s_pick, 1)

            def step(g):
                first = g.known and g.g == 0
                last = g.known and g.g + 1 == GROUPS
                if not first:
                    copy_q(g.next(-1))
                if not last:
                    make_pick(g.next(1))
                find_same(g)
                if not last:
                    copy_xs(g.next(1))
                find_repeats(g)
                if not first:
                    place_sums(g.next(-1))
                    copy_sum(g.next(-1))

            make_pick(Group(0, 0))
            copy_xs(Group(0, 0))
            groups(dve, step)
            for finish in (copy_q, place_sums, copy_sum):
                finish(Group(FULL // 4, FULL % 4))

            def moments_of(b, half, quarter, s, s4, p, r, n0):
                wait(dve, s_upd_mm, b + 1)
                wait(dve, s_base, b + 1)
                wait(dve, s_y_out, b - 3)
                wait(dve, s_y_out_act, b - 3)
                nc.vector.scalar_tensor_tensor(out=y[s4][0:p, 0:r * D], in0=base[s4][0:p, 0:r * D], scalar=2.0,
                                               in1=psum[2 + s][0:p, 0:r * D], op0=ALU.mult, op1=ALU.add
                                               ).then_inc(s_y, 1)
                dve.wait_ge(s_y, b + 1)
                for j in range(r):
                    last = nc.vector.bn_stats(stats[s4][0:p, j, :], y[s4][0:p, j * D:(j + 1) * D])
                last.then_inc(s_stats, 1)
                dve.wait_ge(s_half_n2, 1)
                dve.wait_ge(s_stats, b + 1)
                for j in range(r):
                    last = nc.vector.bn_aggr(moments[s4][0:p, j, :], stats[s4][0:p, j, :])
                last.then_inc(s_moments, 1)
                dve.wait_ge(s_moments, b + 1)
                nc.vector.tensor_scalar(var_eps[s4][0:p, 0:r], moments[s4][0:p, 0:r, 1], EPS, None, ALU.add
                                        ).then_inc(s_var_eps, 1)

            def normalise(b, half, quarter, s, s4, p, r, n0):
                dve.wait_ge(s_rstd, b + 1)
                nc.vector.scalar_tensor_tensor(out=shift[s4][0:p, 0:r], in0=moments[s4][0:p, 0:r, 0], scalar=-1.0,
                                               in1=rstd[s4][0:p, 0:r], op0=ALU.mult, op1=ALU.mult).then_inc(s_shift, 1)
                wait(dve, s_out[s4], quarter * 16)
                for j in range(dve_rows(r)):
                    last = nc.vector.tensor_scalar(y_out[s4][0:p, j * D:(j + 1) * D], y[s4][0:p, j * D:(j + 1) * D],
                                                   moments[s4][0:p, j, 0:1], rstd[s4][0:p, j:j + 1],
                                                   ALU.subtract, ALU.mult)
                last.then_inc(s_y_out, 1)

            blocks_staggered(dve, moments_of, normalise)


def kernel(**inputs):
    import numpy as np
    import concourse.bacc as bacc
    from concourse.bass_utils import run_bass_kernel_spmd

    a = {k: np.asarray(v) for k, v in inputs.items()}
    x, src, dst = a["x"], a["src"], a["dst"]
    N, E = x.shape[0], src.shape[0]
    full, last_tiles, last_p = edge_split(E)

    def by_partition(idx):
        o = np.zeros((full + 1, P, TILES), idx.dtype)
        o[:full] = idx[:full * GROUP].reshape(full, TILES, P).transpose(0, 2, 1)
        o[full, :last_p, :last_tiles] = idx[full * GROUP:].reshape(last_tiles, last_p).T
        return o

    blocks, ends = node_split(N)
    parts, n0 = [], 0
    for p, r in [(P, ROWS)] * blocks + ends:
        parts.append(x[n0:n0 + p * r].reshape(p, r, D).transpose(2, 1, 0).reshape(D, p * r))
        n0 += p * r
    eW1, nW1 = a["L0_gnn_eW1"], a["L0_gnn_nW1"]
    arrays = {
        "x_d": x, "xT_d": np.concatenate(parts, axis=1), "src_d": src, "dst_d": dst,
        "gather_idx_d": np.concatenate([by_partition(src), by_partition(dst)], axis=2),
        "attrT_d": a["edge_attr_16"].T,
        "w1s_d": eW1[:D], "w1d_d": eW1[D:2 * D], "w1a_d": eW1[2 * D:], "eb1_d": a["L0_gnn_eb1"],
        "w2_d": a["L0_gnn_eW2"], "eb2_d": a["L0_gnn_eb2"],
        "nw1a_d": nW1[:D], "nb1_d": a["L0_gnn_nb1"], "nw1b_d": nW1[D:],
        "nw2_d": a["L0_gnn_nW2"], "nb2_d": a["L0_gnn_nb2"],
    }
    arrays = {k: np.ascontiguousarray(v) for k, v in arrays.items()}
    nc = bacc.Bacc("TRN2", target_bir_lowering=False, num_devices=1)
    args = [nc.dram_tensor(k, v.shape, mybir.dt.from_np(v.dtype), kind="ExternalInput").ap() for k, v in arrays.items()]
    out = nc.dram_tensor("out", (N, D), F32, kind="ExternalOutput").ap()
    gnn_kernel(nc, *args, out)
    r = run_bass_kernel_spmd(nc, [arrays], core_ids=[0])
    return r.results[0]["out"]
```
